# Optimizing a Trainium2 kernel written in Bass

```python
import numpy as np
import jax
import jax.numpy as jnp

def _softmax(x, axis=-1):
    return jax.nn.softmax(x, axis=axis)

def _gelu(x):
    return jax.nn.gelu(x, approximate=True)

def _silu(x):
    return jax.nn.silu(x)

def _sigmoid(x):
    return jax.nn.sigmoid(x)

def _layernorm(x, axis=-1, eps=1e-05):
    m = jnp.mean(x, axis=axis, keepdims=True)
    v = jnp.var(x, axis=axis, keepdims=True)
    return (x - m) / jnp.sqrt(v + eps)

def _scatter_add(tgt, idx, src, axis=0):
    return tgt.at[idx].add(src)

def _segment_sum(src, seg, n):
    return jax.ops.segment_sum(src, seg, n)
kernel_name = 'mk_xattn_seq_d1_seqx_r2_07db13'

def setup_inputs(seed: int=0):
    np.random.seed(seed)
    _w = jnp.asarray

    def _rec_inputs():
        import jax
        import jax.numpy as jnp
        _rk = jax.random.key(seed)
        x = -7.109e-05 + 0.9999 * jax.random.normal(jax.random.fold_in(_rk, 1), (8, 224, 512), jnp.float32)
        _lenS = 224 - jax.random.randint(jax.random.fold_in(_rk, 7), (8,), 0, max(1, 224 // 4) + 1, jnp.int32)
        _lenS2 = 750 - jax.random.randint(jax.random.fold_in(_rk, 8), (8,), 0, max(1, 750 // 4) + 1, jnp.int32)
        _ctx_1024P = jax.random.normal(jax.random.fold_in(_rk, 11), (8, 16, 512), jnp.float32)
        _ctx_1024c = jax.random.dirichlet(jax.random.fold_in(_rk, 511), 0.3 * jnp.ones((16,), jnp.float32), (8, 750))
        _ctx_1024t = jnp.einsum('bsk,bkd->bsd', _ctx_1024c, _ctx_1024P)
        _ctx_1024t = _ctx_1024t * jax.lax.rsqrt(jnp.mean(jnp.square(_ctx_1024t)) + 1e-12) * 0.953939
        ctx_1024 = -5.72187e-05 + 0.999849 * (_ctx_1024t + 0.3 * jax.random.normal(jax.random.fold_in(_rk, 611), (8, 750, 512), jnp.float32))
        return (x, ctx_1024)
    x, ctx_1024 = _rec_inputs()

    def _L0_xattn_setup():
        import jax, jax.numpy as jnp
        import numpy as np
        TOPK = 10
        NUM_HEADS = 16
        key = jax.random.key(seed)
        ks = jax.random.split(key, 8)
        B, N, S, D = (32, 1024, 1024, 512)
        sc = 1.0 / np.sqrt(D)
        return {'base_hidden': jax.random.normal(ks[0], (B, N, D), jnp.float32), 'scaffold_hidden': jax.random.normal(ks[1], (B, S, D), jnp.float32), 'in_proj_w': jax.random.normal(ks[2], (3 * D, D), jnp.float32) * sc, 'in_proj_b': jax.random.normal(ks[3], (3 * D,), jnp.float32) * 0.02, 'out_w': jax.random.normal(ks[4], (D, D), jnp.float32) * sc, 'out_b': jax.random.normal(ks[5], (D,), jnp.float32) * 0.02, 'score_w': jax.random.normal(ks[6], (1, D), jnp.float32) * sc, 'score_b': jax.random.normal(ks[7], (1,), jnp.float32) * 0.02}
    _L0_xattn_all = _L0_xattn_setup()
    _L0_xattn_in = {k: v for k, v in _L0_xattn_all.items() if k in ('in_proj_w', 'in_proj_b', 'out_w', 'out_b', 'score_w', 'score_b')}
    del _L0_xattn_all
    return {'x': x, 'ctx_1024': ctx_1024, 'L0_xattn_in_proj_w': _L0_xattn_in['in_proj_w'], 'L0_xattn_in_proj_b': _L0_xattn_in['in_proj_b'], 'L0_xattn_out_w': _L0_xattn_in['out_w'], 'L0_xattn_out_b': _L0_xattn_in['out_b'], 'L0_xattn_score_w': _L0_xattn_in['score_w'], 'L0_xattn_score_b': _L0_xattn_in['score_b']}

def reference(x, ctx_1024, L0_xattn_in_proj_w, L0_xattn_in_proj_b, L0_xattn_out_w, L0_xattn_out_b, L0_xattn_score_w, L0_xattn_score_b):
    import jax
    import jax.numpy as jnp

    def _L0_xattn_ref(base_hidden, scaffold_hidden, in_proj_w, in_proj_b, out_w, out_b, score_w, score_b):
        import jax, jax.numpy as jnp
        import numpy as np
        TOPK = 10
        NUM_HEADS = 16
        B, N, D = base_hidden.shape
        H = NUM_HEADS
        dh = D // H
        scores = jnp.einsum('bnd,d->bn', base_hidden, score_w[0]) + score_b[0]
        _, topk_idx = jax.lax.top_k(scores, TOPK)
        sparse_hidden = jnp.take_along_axis(base_hidden, topk_idx[:, :, None], axis=1)
        Wq, Wk, Wv = jnp.split(in_proj_w, 3, axis=0)
        bq, bk, bv = jnp.split(in_proj_b, 3)
        q = (sparse_hidden @ Wq.T + bq).reshape(B, TOPK, H, dh).transpose(0, 2, 1, 3)
        k = (scaffold_hidden @ Wk.T + bk).reshape(B, -1, H, dh).transpose(0, 2, 1, 3)
        v = (scaffold_hidden @ Wv.T + bv).reshape(B, -1, H, dh).transpose(0, 2, 1, 3)
        scale = 1.0 / np.sqrt(dh).astype(np.float32)
        logits = jnp.einsum('bhqd,bhkd->bhqk', q, k) * scale
        attn = jax.nn.softmax(logits, axis=-1)
        o = jnp.einsum('bhqk,bhkd->bhqd', attn, v).transpose(0, 2, 1, 3).reshape(B, TOPK, D)
        attn_out = o @ out_w.T + out_b
        return base_hidden.at[jnp.arange(B)[:, None], topk_idx].set(attn_out)
    x = _L0_xattn_ref(x, ctx_1024, L0_xattn_in_proj_w, L0_xattn_in_proj_b, L0_xattn_out_w, L0_xattn_out_b, L0_xattn_score_w, L0_xattn_score_b)
    return x

_drawn_inputs = setup_inputs


def setup_inputs(seed=0):
    import zlib

    import numpy as np

    out = dict(_drawn_inputs(seed))
    spreads = {}
    factors = {'L0_xattn_in_proj_b': 8.0, 'L0_xattn_out_b': 8.0}
    for name, (base, spread) in spreads.items():
        noise = np.random.default_rng([zlib.crc32(name.encode()), seed]).standard_normal(out[name].shape)
        drawn = base * np.exp(spread * noise) if base else spread * noise
        out[name] = jnp.asarray(drawn.astype(out[name].dtype))
    for name, factor in factors.items():
        out[name] = (out[name] * factor).astype(out[name].dtype)
    return out
```

```python
from contextlib import ExitStack

import concourse.bass as bass
from concourse import mybir

F32 = mybir.dt.float32
I32 = mybir.dt.int32
U32 = mybir.dt.uint32
ALU = mybir.AluOpType
ACT = mybir.ActivationFunctionType
AX = mybir.AxisListType
RMAX = bass.bass_isa.ReduceOp.max

B, N, D, S = 8, 224, 512, 750
HEADS, TOPK = 16, 10
DH = D // HEADS
P = 128
DT = D // P
HPT = P // DH
S_T = 6
S_P = S // S_T
BANK_T = S_T // 2
X_P = N // 2
HQ = HEADS * TOPK
GROUPS = 2
GB = B // GROUPS
GQ = GB * TOPK
BQ = B * TOPK
SCALE = float(DH) ** -0.5
LOWEST = -3.4028234663852886e38
QK_STEPS = DT + 1
QK_UNITS = 2 * QK_STEPS
CTX_MAIN = 120


def build(nc, x, ctx_rows, ctx_cols, wq, wk, wv, wo, in_bias, out_b, score_w, score_b, out):
    x_rows = x.rearrange("b n d -> (b n) d")
    out_rows = out.rearrange("b n d -> (b n) d")
    x_pairs = x.rearrange("b (p j) d -> p b j d", j=2)
    out_pairs = out.rearrange("b (p j) d -> p b j d", j=2)

    stack = ExitStack()
    with stack:
        def sb(name, shape, dt=F32):
            return stack.enter_context(nc.sbuf_tensor(name, shape, dt))

        def ps(name, shape):
            return stack.enter_context(nc.psum_tensor(name, shape, F32))

        def sem(name):
            return stack.enter_context(nc.semaphore(name))

        x_sb = sb("x_sb", [X_P, B, 2, D])
        wq_sb = sb("wq_sb", [P, DT, D])
        wk_sb = sb("wk_sb", [P, DT, D])
        wv_sb = sb("wv_sb", [P, DT, D])
        wo_sb = sb("wo_sb", [P, DT, D])
        bias_sb = sb("bias_sb", [P, 3, DT])
        out_b_sb = sb("out_b_sb", [GQ, D])
        score_w_sb = sb("score_w_sb", [X_P, D])
        score_b_sb = sb("score_b_sb", [GB, 1])
        ctx_c = [sb(f"ctx_c{n}", [P, DT, S_T, S_P]) for n in range(2)]
        ctx_r = [sb(f"ctx_r{n}", [S_P, S_T, D]) for n in range(2)]
        ident = sb("ident", [P, P])
        ones = sb("ones", [P, P])
        own_batch = sb("own_batch", [GB, GB, TOPK])
        row_base_i = sb("row_base_i", [GB, GROUPS], I32)
        row_base = sb("row_base", [GB, GROUPS])
        products = [sb(f"product{j}", [X_P, D]) for j in range(2)]
        scores = sb("scores", [X_P, 2, B])
        score_rows = sb("score_rows", [GB, N])
        score_rest = sb("score_rest", [GB, N])
        top = sb("top", [GB, 16])
        top_idx = sb("top_idx", [GB, 16], U32)
        idx_diag = sb("idx_diag", [GB, GB, TOPK])
        row_idx = [sb(f"row_idx{g}", [GQ, 1], U32) for g in range(GROUPS)]
        picked = [sb(f"picked{g}", [GQ, D]) for g in range(GROUPS)]
        picked_T = sb("picked_T", [P, DT, GQ])
        key_bias = sb("key_bias", [P, DT, P])
        q_diag = sb("q_diag", [P, DT, GB, HPT, TOPK])
        qk = sb("qk", [P, B, QK_STEPS, HQ])
        col_max = sb("col_max", [S_P, HQ])
        all_max = sb("all_max", [S_P, HQ])
        shift = sb("shift", [S_P, HQ])
        probs = [sb(f"probs{n}", [S_P, S_T, HQ]) for n in range(2)]
        prob_sum = [sb(f"prob_sum{n}", [S_P, HQ]) for n in range(2)]
        inv_sum = sb("inv_sum", [P, HQ])
        mix = sb("mix", [P, DT, HEADS, BQ])
        o_T = sb("o_T", [P, DT, BQ])
        y_sb = [sb(f"y_sb{g}", [GQ, D]) for g in range(GROUPS)]

        logits_ps = [ps(f"logits_ps{n}", [P, 2, 512]) for n in range(2)]
        mix_ps = [ps(f"mix_ps{n}", [P, 512]) for n in range(2)]
        misc_ps = [ps(f"misc_ps{n}", [P, 512]) for n in range(2)]

        x_in = [sem(f"x_in{b}") for b in range(B)]
        score_w_in, small_in = sem("score_w_in"), sem("small_in")
        wq_in, wk_in, wv_in, wo_in = sem("wq_in"), sem("wk_in"), sem("wv_in"), sem("wo_in")
        ctx_c_in = [sem(f"ctx_c_in{n}") for n in range(2)]
        ctx_r_in = [sem(f"ctx_r_in{n}") for n in range(2)]
        consts_cleared, consts_done, vec_consts = sem("consts_cleared"), sem("consts_done"), sem("vec_consts")
        scored, scores_T, topk_step = sem("scored"), sem("scores_T"), sem("topk_step")
        idx_diag_done, idx_moved, idx_ready = sem("idx_diag_done"), sem("idx_moved"), sem("idx_ready")
        gathered = [sem(f"gathered{g}") for g in range(GROUPS)]
        picked_T_ps, picked_T_done = sem("picked_T_ps"), sem("picked_T_done")
        q_ps, q_done = sem("q_ps"), sem("q_done")
        qk_ps, qk_done = sem("qk_ps"), sem("qk_done")
        logits_done, max_done, max_step, shift_done = sem("logits_done"), sem("max_done"), sem("max_step"), sem("shift_done")
        shifted, exp_done, sum_done, den_done = sem("shifted"), sem("exp_done"), sem("sum_done"), sem("den_done")
        inv_done = sem("inv_done")
        mix_ready = [sem(f"mix_ready{n}") for n in range(2)]
        mix_out = [sem(f"mix_out{n}") for n in range(2)]
        o_ps, o_done, y_ps, y_done = sem("o_ps"), sem("o_done"), sem("y_ps"), sem("y_done")
        x_copied, scattered = sem("x_copied"), sem("scattered")

        block = stack.enter_context(nc.Block())

        @block.sync
        def _(sp):
            def load_cols(b, n):
                sp.dma_start(ctx_c[n][:, :, :, :], ctx_cols[b, :, :, :, :]).then_inc(ctx_c_in[n], 16)

            def load_rows(b, n):
                sp.dma_start(ctx_r[n][0:CTX_MAIN, :, :], ctx_rows[b, 0:CTX_MAIN, :, :]).then_inc(ctx_r_in[n], 16)
                sp.dma_start(ctx_r[n][CTX_MAIN:S_P, :, :], ctx_rows[b, CTX_MAIN:S_P, :, :]).then_inc(ctx_r_in[n], 16)

            for b in range(GB):
                sp.dma_start(x_sb[:, b, :, :], x_pairs[:, b, :, :]).then_inc(x_in[b], 16)
            sp.dma_start(wq_sb[:, :, :], wq).then_inc(wq_in, 16)
            for b in range(GB, B):
                sp.dma_start(x_sb[:, b, :, :], x_pairs[:, b, :, :]).then_inc(x_in[b], 16)
            sp.dma_start(wk_sb[:, :, :], wk).then_inc(wk_in, 16)
            load_cols(0, 0)
            load_cols(1, 1)
            load_rows(0, 0)
            load_rows(1, 1)
            for b in range(B):
                sp.wait_ge(x_in[b], 16)
                sp.dma_start(out_pairs[:, b, :, :], x_sb[:, b, :, :]).then_inc(x_copied, 16)
            sp.dma_start(wv_sb[:, :, :], wv).then_inc(wv_in, 16)
            sp.dma_start(wo_sb[:, :, :], wo).then_inc(wo_in, 16)
            with sp.Fori(0, B // 2 - 1) as i:
                for n in range(2):
                    b = i * 2 + (2 + n)
                    sp.wait_ge(logits_done, i * 2 + (1 + n))
                    load_cols(b, n)
                    sp.wait_ge(mix_ready[1], i * 2 + (1 + n))
                    load_rows(b, n)
            sp.wait_ge(scattered, 16 * GROUPS)

        @block.gpsimd
        def _(pool):
            pool.memset(ident[:, :], 0.0).then_inc(consts_cleared, 1)
            pool.memset(own_batch[:, :, :], 0.0).then_inc(consts_cleared, 1)
            pool.wait_ge(consts_cleared, 2)
            pool.affine_select(out=ident[:, :], in_=ident[:, :], compare_op=ALU.not_equal, fill=1.0,
                               base=0, pattern=[[-1, P]], channel_multiplier=1).then_inc(consts_done, 1)
            pool.affine_select(out=own_batch[:, :, :], in_=own_batch[:, :, :], compare_op=ALU.not_equal, fill=1.0,
                               base=0, pattern=[[-1, GB], [0, TOPK]], channel_multiplier=1).then_inc(consts_done, 1)
            pool.iota(row_base_i[:, :], pattern=[[GB * N, GROUPS]], base=0, channel_multiplier=N).then_inc(consts_done, 1)
            for g in range(GROUPS):
                pool.wait_ge(idx_ready, g + 1)
                pool.indirect_dma_start(out=picked[g][:, :], out_offset=None, in_=x_rows,
                                        in_offset=bass.IndirectOffsetOnAxis(ap=row_idx[g][:, 0:1], axis=0))\
                    .then_inc(gathered[g], 16)
            pool.wait_ge(qk_done, QK_UNITS)
            for b in range(B):
                pool.wait_ge(max_done, b + 1)
                pool.wait_ge(shifted, b)
                pool.tensor_tensor(col_max[:, :], col_max[:, :], qk[0:S_P, b, DT, :], ALU.add).then_inc(max_step, 1)
                pool.wait_ge(max_step, b * 2 + 1)
                pool.partition_all_reduce(all_max[:, :], col_max[:, :], S_P, RMAX).then_inc(max_step, 1)
                pool.wait_ge(max_step, b * 2 + 2)
                pool.tensor_tensor(shift[:, :], qk[0:S_P, b, DT, :], all_max[:, :], ALU.subtract).then_inc(shift_done, 1)
            pool.wait_ge(x_copied, 16 * B)
            for g in range(GROUPS):
                pool.wait_ge(y_done, g + 1)
                pool.indirect_dma_start(out=out_rows, out_offset=bass.IndirectOffsetOnAxis(ap=row_idx[g][:, 0:1], axis=0),
                                        in_=y_sb[g][:, :], in_offset=None).then_inc(scattered, 16)

        @block.scalar
        def _(act):
            act.dma_start(score_w_sb[:, :], score_w.broadcast_to([X_P, D])).then_inc(score_w_in, 16)
            act.dma_start(score_b_sb[:, :], score_b.broadcast_to([GB, 1])).then_inc(small_in, 16)
            act.dma_start(bias_sb[:, :, :], in_bias).then_inc(small_in, 16)
            act.dma_start(out_b_sb[:, :], out_b.broadcast_to([GQ, D])).then_inc(small_in, 16)
            for g in range(GROUPS):
                act.wait_ge(picked_T_ps, g + 1)
                if g:
                    act.wait_ge(q_ps, g)
                nc.scalar.activation(picked_T[:, :, :], misc_ps[1][:, 0:DT * GQ].rearrange("p (t q) -> p t q", t=DT),
                                     ACT.Copy).then_inc(picked_T_done, 1)
                for u in range(QK_UNITS):
                    step, half = u // 2, u % 2
                    act.wait_ge(qk_ps, g * QK_UNITS + u + 1)
                    nc.scalar.activation(
                        qk[:, g * GB:(g + 1) * GB, step, half * 2 * GQ:(half + 1) * 2 * GQ].rearrange("p b (e c) -> p e b c", e=2),
                        misc_ps[u % 2][:, 0:2 * HQ].rearrange("p (e b c) -> p e b c", e=2, b=GB),
                        ACT.Copy).then_inc(qk_done, 1)
            with act.Fori(0, B // 2) as i:
                for n in range(2):
                    act.wait_ge(shifted, i * 2 + (n + 1))
                    nc.scalar.activation(probs[n][:, :, :], probs[n][:, :, :], ACT.Exp, scale=SCALE).then_inc(exp_done, 1)

        @block.vector
        def _(dve):
            def score(b):
                dve.wait_ge(x_in[b], 16)
                for j in range(2):
                    if b:
                        dve.wait_ge(scored, 2 * b + j - 1)
                    nc.vector.tensor_tensor_reduce(
                        out=products[j][:, :], in0=x_sb[:, b, j, :], in1=score_w_sb[:, :], scale=1.0, scalar=0.0,
                        op0=ALU.mult, op1=ALU.add, accum_out=scores[:, j, b:b + 1]).then_inc(scored, 1)

            def choose(g):
                steps = [0]

                def link(ins):
                    steps[0] += 1
                    ins.then_inc(topk_step, 1)
                    dve.wait_ge(topk_step, 6 * g + steps[0])

                dve.wait_ge(scores_T, g + 1)
                link(nc.vector.tensor_scalar(
                    score_rows[:, :].rearrange("b (p j) -> b j p", j=2),
                    mix_ps[0][0:GB, 0:N].rearrange("b (j p) -> b j p", j=2), score_b_sb[:, 0:1], None, ALU.add))
                link(nc.vector.max(top[:, 0:8], score_rows[:, :]))
                link(nc.vector.max_index(top_idx[:, 0:8], top[:, 0:8], score_rows[:, :]))
                link(nc.vector.match_replace(score_rest[:, :], top[:, 0:8], score_rows[:, :], LOWEST))
                link(nc.vector.max(top[:, 8:16], score_rest[:, :]))
                link(nc.vector.max_index(top_idx[:, 8:16], top[:, 8:16], score_rest[:, :]))
                nc.vector.scalar_tensor_tensor(
                    out=idx_diag[:, :, :], in0=top_idx[:, 0:TOPK].unsqueeze(1).broadcast_to([GB, GB, TOPK]),
                    scalar=row_base[:, g:g + 1], in1=own_batch[:, :, :], op0=ALU.add, op1=ALU.mult)\
                    .then_inc(idx_diag_done, 1)

            def move_idx(g):
                dve.wait_ge(idx_moved, g + 1)
                nc.vector.tensor_copy(row_idx[g][:, :], mix_ps[1][0:GQ, 0:1]).then_inc(idx_ready, 1)

            def spread_queries(g):
                dve.wait_ge(q_ps, g + 1)
                if g:
                    dve.wait_ge(qk_ps, g * QK_UNITS)
                for h in range(HPT):
                    rows = slice(h * DH, (h + 1) * DH)
                    last = nc.vector.tensor_tensor(
                        q_diag[rows, :, :, h, :],
                        misc_ps[0][rows, 0:DT * GQ].rearrange("p (t b q) -> p t b q", t=DT, b=GB),
                        bias_sb[rows, 0, :].unsqueeze(2).unsqueeze(3).broadcast_to([DH, DT, GB, TOPK]), ALU.add)
                last.then_inc(q_done, 1)

            def tiles(n):
                return logits_ps[n][0:S_P, :, 0:BANK_T * HQ].rearrange("p k (t c) -> p k t c", t=BANK_T)

            def find_max(b, n):
                dve.wait_ge(logits_done, b + 1)
                nc.vector.tensor_reduce(col_max[:, :], tiles(n).rearrange("p k t c -> p c k t"), AX.XY, ALU.max)\
                    .then_inc(max_done, 1)

            def subtract_max(b, n, waits_mix):
                dve.wait_ge(shift_done, b + 1)
                if waits_mix:
                    dve.wait_ge(mix_ready[1], b - 1)
                nc.vector.tensor_tensor(
                    probs[n][:, :, :].rearrange("p (k t) c -> p k t c", k=2), tiles(n),
                    shift[:, :].unsqueeze(1).unsqueeze(2).broadcast_to([S_P, 2, BANK_T, HQ]), ALU.add)\
                    .then_inc(shifted, 1)

            def sum_probs(b, n, waits_den):
                dve.wait_ge(exp_done, b + 1)
                if waits_den:
                    dve.wait_ge(den_done, b - 1)
                nc.vector.tensor_reduce(prob_sum[n][:, :], probs[n][:, :, :].rearrange("p t c -> p c t"), AX.X, ALU.add)\
                    .then_inc(sum_done, 1)

            def invert(b):
                dve.wait_ge(den_done, b + 1)
                dve.wait_ge(mix_out[1], b)
                nc.vector.reciprocal(inv_sum[:, :], misc_ps[0][:, 0:HQ]).then_inc(inv_done, 1)

            def normalise(b, half):
                dve.wait_ge(inv_done, b + 1)
                dve.wait_ge(mix_ready[half], b + 1)
                nc.vector.tensor_tensor(
                    mix[:, 2 * half:2 * half + 2, :, bass.ds(b * TOPK, TOPK)],
                    mix_ps[half][:, 0:2 * HQ].rearrange("p (t h q) -> p t h q", t=2, h=HEADS),
                    inv_sum[:, :].rearrange("p (h q) -> p h q", h=HEADS).unsqueeze(1).broadcast_to([P, 2, HEADS, TOPK]),
                    ALU.mult).then_inc(mix_out[half], 1)

            def batch(b, n, waits=True):
                find_max(b, n)
                invert(b - 1)
                normalise(b - 1, 0)
                subtract_max(b, n, waits)
                normalise(b - 1, 1)
                sum_probs(b, n, waits)

            def finish_heads(k, c0, c1):
                dve.wait_ge(o_ps, k + 1)
                nc.vector.tensor_tensor(
                    o_T[:, :, c0:c1], misc_ps[1][:, 0:DT * (c1 - c0)].rearrange("p (t q) -> p t q", t=DT),
                    bias_sb[:, 2, :].unsqueeze(2).broadcast_to([P, DT, c1 - c0]), ALU.add).then_inc(o_done, 1)

            def finish_output(g):
                dve.wait_ge(y_ps, g + 1)
                nc.vector.tensor_tensor(y_sb[g][:, :], logits_ps[0][0:GQ, g, :], out_b_sb[:, :], ALU.add)\
                    .then_inc(y_done, 1)

            nc.vector.memset(q_diag[:, :, :, :, :], 0.0).then_inc(vec_consts, 1)
            nc.vector.memset(ones[:, :], 1.0).then_inc(vec_consts, 1)
            dve.wait_ge(consts_done, 3)
            nc.vector.tensor_copy(row_base[:, :], row_base_i[:, :]).then_inc(vec_consts, 1)
            dve.wait_ge(score_w_in, 16)
            for b in range(GB):
                score(b)
            dve.wait_ge(small_in, 48)
            dve.wait_ge(vec_consts, 3)
            choose(0)
            nc.vector.tensor_copy(key_bias[:, :, :], bias_sb[:, 1, :].unsqueeze(2).broadcast_to([P, DT, P]))\
                .then_inc(vec_consts, 1)
            move_idx(0)
            for b in range(GB, B):
                score(b)
            spread_queries(0)
            choose(1)
            move_idx(1)
            find_max(0, 0)
            spread_queries(1)
            subtract_max(0, 0, False)
            sum_probs(0, 0, False)
            with dve.Fori(0, B // 2 - 1) as i:
                batch(i * 2 + 1, 1)
                batch(i * 2 + 2, 0)
            batch(B - 1, 1)
            finish_heads(0, 0, BQ - TOPK)
            finish_output(0)
            invert(B - 1)
            normalise(B - 1, 0)
            normalise(B - 1, 1)
            finish_heads(1, BQ - TOPK, BQ)
            finish_output(1)

        @block.tensor
        def _(pe):
            def transpose_scores(g):
                pe.wait_ge(scored, 2 * GB * (g + 1))
                if g:
                    pe.wait_ge(topk_step, 6 * g)
                for j in range(2):
                    last = nc.tensor.transpose(mix_ps[0][0:GB, j * X_P:(j + 1) * X_P],
                                               scores[:, j, g * GB:(g + 1) * GB], ident[0:X_P, 0:X_P])
                last.then_inc(scores_T, 1)

            def move_idx(g):
                pe.wait_ge(idx_diag_done, g + 1)
                if g:
                    pe.wait_ge(idx_ready, g)
                nc.tensor.matmul(mix_ps[1][0:GQ, 0:1], idx_diag[:, :, :].rearrange("k b q -> k (b q)"),
                                 ones[0:GB, 0:1], start=True, stop=True).then_inc(idx_moved, 1)

            def transpose_picked(g):
                pe.wait_ge(gathered[g], 16)
                if g:
                    pe.wait_ge(qk_done, g * QK_UNITS)
                for t in range(DT):
                    last = nc.tensor.transpose(misc_ps[1][:, t * GQ:(t + 1) * GQ],
                                               picked[g][:, t * P:(t + 1) * P], ident[0:GQ, 0:GQ])
                last.then_inc(picked_T_ps, 1)

            def project_queries(g):
                pe.wait_ge(picked_T_done, g + 1)
                for e in range(DT):
                    for t in range(DT):
                        last = nc.tensor.matmul(misc_ps[0][:, e * GQ:(e + 1) * GQ], wq_sb[:, t, e * P:(e + 1) * P],
                                                picked_T[:, t, :], start=(t == 0), stop=(t == DT - 1))
                last.then_inc(q_ps, 1)

            def fold_keys(g):
                pe.wait_ge(q_done, g + 1)
                for u in range(QK_UNITS):
                    step, half = u // 2, u % 2
                    if u >= 2:
                        pe.wait_ge(qk_done, g * QK_UNITS + u - 1)
                    for k in range(2):
                        e = 2 * half + k
                        w = wk_sb[:, e, step * P:(step + 1) * P] if step < DT else key_bias[:, e, :]
                        last = nc.tensor.matmul(misc_ps[u % 2][:, k * HQ:(k + 1) * HQ], w,
                                                q_diag[:, e, :, :, :].rearrange("p b h q -> p (b h q)"),
                                                start=True, stop=True)
                    last.then_inc(qk_ps, 1)

            def logits(b, n, use, waits_slot):
                pe.wait_ge(ctx_c_in[n], use * 16 + 16)
                if waits_slot:
                    pe.wait_ge(shifted, b - 1)
                for t in range(S_T):
                    for f in range(DT):
                        last = nc.tensor.matmul(
                            logits_ps[n][0:S_P, t // BANK_T, (t % BANK_T) * HQ:(t % BANK_T + 1) * HQ],
                            ctx_c[n][:, f, t, :], qk[:, b, f, :], start=(f == 0), stop=(f == DT - 1))
                last.then_inc(logits_done, 1)

            def weigh(b, n, use):
                pe.wait_ge(ctx_r_in[n], use * 32 + 32)
                pe.wait_ge(exp_done, b + 1)
                for half in range(2):
                    pe.wait_ge(mix_out[half], b)
                    for f in range(2):
                        for t in range(S_T):
                            c = (2 * half + f) * P
                            last = nc.tensor.matmul(mix_ps[half][:, f * HQ:(f + 1) * HQ], ctx_r[n][:, t, c:c + P],
                                                    probs[n][:, t, :], start=(t == 0), stop=(t == S_T - 1))
                    last.then_inc(mix_ready[half], 1)
                    if half == 0:
                        pe.wait_ge(sum_done, b + 1)
                        pe.wait_ge(inv_done, b)
                        nc.tensor.matmul(misc_ps[0][:, 0:HQ], ones[0:S_P, :], prob_sum[n][:, :],
                                         start=True, stop=True).then_inc(den_done, 1)

            def project_values(k, b0, b1):
                for half in range(2):
                    pe.wait_ge(mix_out[half], b1)
                w = (b1 - b0) * TOPK
                if k:
                    pe.wait_ge(o_done, k)
                for e in range(DT):
                    for t in range(DT):
                        for h in range(HPT):
                            c = e * P + h * DH
                            last = nc.tensor.matmul(misc_ps[1][h * DH:(h + 1) * DH, e * w:(e + 1) * w],
                                                    wv_sb[:, t, c:c + DH], mix[:, t, e * HPT + h, b0 * TOPK:b1 * TOPK],
                                                    start=(t == 0), stop=(t == DT - 1), skip_group_check=True)
                last.then_inc(o_ps, 1)

            def project_output(g):
                for e in range(DT):
                    last = nc.tensor.matmul(logits_ps[0][0:GQ, g, :], o_T[:, e, g * GQ:(g + 1) * GQ], wo_sb[:, e, :],
                                            start=(e == 0), stop=(e == DT - 1))
                last.then_inc(y_ps, 1)

            pe.wait_ge(consts_done, 2)
            pe.wait_ge(vec_consts, 2)
            transpose_scores(0)
            move_idx(0)
            transpose_picked(0)
            pe.wait_ge(wq_in, 16)
            project_queries(0)
            transpose_scores(1)
            pe.wait_ge(wk_in, 16)
            pe.wait_ge(vec_consts, 4)
            fold_keys(0)
            move_idx(1)
            pe.wait_ge(qk_done, QK_UNITS)
            logits(0, 0, 0, False)
            transpose_picked(1)
            project_queries(1)
            fold_keys(1)
            pe.wait_ge(qk_done, 2 * QK_UNITS)
            with pe.Fori(0, B // 2 - 1) as i:
                logits(i * 2 + 1, 1, i, True)
                weigh(i * 2, 0, i)
                logits(i * 2 + 2, 0, i + 1, True)
                weigh(i * 2 + 1, 1, i)
            logits(B - 1, 1, B // 2 - 1, True)
            weigh(B - 2, 0, B // 2 - 1)
            pe.wait_ge(wv_in, 16)
            project_values(0, 0, B - 1)
            pe.wait_ge(wo_in, 16)
            pe.wait_ge(o_done, 1)
            project_output(0)
            weigh(B - 1, 1, B // 2 - 1)
            project_values(1, B - 1, B)
            pe.wait_ge(o_done, 2)
            project_output(1)


def kernel(x, ctx_1024, L0_xattn_in_proj_w, L0_xattn_in_proj_b, L0_xattn_out_w, L0_xattn_out_b,
           L0_xattn_score_w, L0_xattn_score_b):
    import numpy as np
    import concourse.bacc as bacc
    from concourse.bass_utils import run_bass_kernel_spmd

    ctx = np.asarray(ctx_1024)
    in_w = np.asarray(L0_xattn_in_proj_w)

    def in_major(w):
        return w.reshape(D, DT, P).transpose(2, 1, 0)

    arrays = {
        "x": np.asarray(x),
        "ctx_rows": ctx.reshape(B, S_P, S_T, D),
        "ctx_cols": ctx.reshape(B, S_P, S_T, DT, P).transpose(0, 4, 3, 2, 1),
        "wq": in_major(in_w[0:D]),
        "wk": in_w[D:2 * D].reshape(DT, P, D).transpose(1, 0, 2),
        "wv": in_major(in_w[2 * D:3 * D]),
        "wo": in_major(np.asarray(L0_xattn_out_w)),
        "in_bias": np.asarray(L0_xattn_in_proj_b).reshape(3, DT, P).transpose(2, 0, 1),
        "out_b": np.asarray(L0_xattn_out_b).reshape(1, D),
        "score_w": np.asarray(L0_xattn_score_w).reshape(1, D),
        "score_b": np.asarray(L0_xattn_score_b).reshape(1, 1),
    }
    nc = bacc.Bacc("TRN2", target_bir_lowering=False, num_devices=1)
    feeds, args = {}, []
    for name, a in arrays.items():
        a = np.ascontiguousarray(a)
        feeds[name + "_dram"] = a
        args.append(nc.dram_tensor(name + "_dram", a.shape, mybir.dt.from_np(a.dtype), kind="ExternalInput").ap())
    out = nc.dram_tensor("out_dram", (B, N, D), F32, kind="ExternalOutput").ap()
    build(nc, *args, out)
    return run_bass_kernel_spmd(nc, [feeds], core_ids=[0]).results[0]["out_dram"]
```

```python
from contextlib import ExitStack

import concourse.bass as bass
from concourse import mybir

F32 = mybir.dt.float32
I32 = mybir.dt.int32
U32 = mybir.dt.uint32
ALU = mybir.AluOpType
ACT = mybir.ActivationFunctionType
AX = mybir.AxisListType
RMAX = bass.bass_isa.ReduceOp.max

B, N, D, S = 8, 224, 512, 750
HEADS, TOPK = 16, 10
DH = D // HEADS
P = 128
DT = D // P
HPT = P // DH
S_T = 6
S_P = S // S_T
BANK_T = S_T // 2
X_P = N // 2
HQ = HEADS * TOPK
GROUPS = [(0, 2), (2, B)]
GB = max(b1 - b0 for b0, b1 in GROUPS)
BQ = B * TOPK
SCALE = float(DH) ** -0.5
LOWEST = -3.4028234663852886e38
QK_STEPS = DT + 1
QK_UNITS = 2 * QK_STEPS
WARM_SCORES, WARM_CHOICE, WARM_GATHER = 11, 14, 18
CTX_MAIN = 120


def build(nc, x, ctx_rows, ctx_cols, wq, wk, wv, wo, in_bias, out_b, score_w, score_b, out):
    x_rows = x.rearrange("b n d -> (b n) d")
    out_rows = out.rearrange("b n d -> (b n) d")
    x_pairs = x.rearrange("b (p j) d -> p b j d", j=2)
    out_pairs = out.rearrange("b (p j) d -> p b j d", j=2)

    stack = ExitStack()
    with stack:
        def sb(name, shape, dt=F32):
            return stack.enter_context(nc.sbuf_tensor(name, shape, dt))

        def ps(name, shape):
            return stack.enter_context(nc.psum_tensor(name, shape, F32))

        def sem(name):
            return stack.enter_context(nc.semaphore(name))

        x_sb = sb("x_sb", [X_P, B, 2, D])
        wq_sb = sb("wq_sb", [P, DT, D])
        wk_sb = sb("wk_sb", [P, DT, D])
        wv_sb = sb("wv_sb", [P, DT, D])
        wo_sb = sb("wo_sb", [P, DT, D])
        bias_sb = sb("bias_sb", [P, 3, DT])
        out_b_sb = sb("out_b_sb", [BQ, D])
        score_w_sb = sb("score_w_sb", [X_P, D])
        score_b_sb = sb("score_b_sb", [GB, 1])
        ctx_c = [sb(f"ctx_c{n}", [P, DT, S_T, S_P]) for n in range(2)]
        ctx_r = [sb(f"ctx_r{n}", [S_P, S_T, D]) for n in range(2)]
        ident = sb("ident", [P, P])
        ones = sb("ones", [P, P])
        own_batch = sb("own_batch", [GB, GB, TOPK])
        row_base_i = sb("row_base_i", [GB, len(GROUPS)], I32)
        row_base = sb("row_base", [GB, len(GROUPS)])
        products = [sb(f"product{j}", [X_P, D]) for j in range(2)]
        scores = sb("scores", [X_P, 2, B])
        score_rows = sb("score_rows", [GB, N])
        score_rest = sb("score_rest", [GB, N])
        top = sb("top", [GB, 16])
        top_idx = sb("top_idx", [GB, 16], U32)
        idx_diag = sb("idx_diag", [GB, len(GROUPS), BQ])
        row_idx = [sb(f"row_idx{g}", [b1 * TOPK, 1], U32) for g, (b0, b1) in enumerate(GROUPS)]
        picked = [sb(f"picked{g}", [b1 * TOPK, D]) for g, (b0, b1) in enumerate(GROUPS)]
        picked_T = [sb(f"picked_T{g}", [P, DT, b1 * TOPK]) for g, (b0, b1) in enumerate(GROUPS)]
        key_bias = sb("key_bias", [P, DT, P])
        q_diag = [sb(f"q_diag{g}", [P, DT, b1 - b0, HPT, TOPK])
                  for g, (b0, b1) in enumerate(GROUPS)]
        qk = sb("qk", [P, B, QK_STEPS, HQ])
        col_max = sb("col_max", [S_P, HQ])
        all_max = sb("all_max", [S_P, HQ])
        shift = sb("shift", [S_P, HQ])
        probs = [sb(f"probs{n}", [S_P, S_T, HQ]) for n in range(2)]
        prob_sum = [sb(f"prob_sum{n}", [S_P, HQ]) for n in range(2)]
        inv_sum = sb("inv_sum", [P, HQ])
        mix = sb("mix", [P, DT, HEADS, BQ])
        o_T = sb("o_T", [P, DT, BQ])
        y_sb = sb("y_sb", [BQ, D])

        logits_ps = [ps(f"logits_ps{n}", [P, 2, 512]) for n in range(2)]
        mix_ps = [ps(f"mix_ps{n}", [P, 512]) for n in range(2)]
        misc_ps = [ps(f"misc_ps{n}", [P, 512]) for n in range(2)]
        heads_ps = [misc_ps[1][:, :], misc_ps[0][:, :], logits_ps[1][:, 0, :], logits_ps[1][:, 1, :]]
        fold_ps = mix_ps + misc_ps

        x_in = [sem(f"x_in{b}") for b in range(B)]
        score_w_in, score_b_in, bias_in, out_b_in = sem("score_w_in"), sem("score_b_in"), sem("bias_in"), sem("out_b_in")
        wq_in, wk_in, wv_in, wo_in = sem("wq_in"), sem("wk_in"), sem("wv_in"), sem("wo_in")
        ctx_c_in = [sem(f"ctx_c_in{n}") for n in range(2)]
        ctx_r_in = [sem(f"ctx_r_in{n}") for n in range(2)]
        consts_cleared, consts_done, vec_consts = sem("consts_cleared"), sem("consts_done"), sem("vec_consts")
        scored, scores_T, topk_step = sem("scored"), sem("scores_T"), sem("topk_step")
        idx_diag_done, idx_moved, idx_ready = sem("idx_diag_done"), sem("idx_moved"), sem("idx_ready")
        gathered = [sem(f"gathered{g}") for g in range(len(GROUPS))]
        picked_T_ps, picked_T_done = sem("picked_T_ps"), sem("picked_T_done")
        q_ps, q_done = sem("q_ps"), sem("q_done")
        qk_ps, qk_done = sem("qk_ps"), sem("qk_done")
        logits_done, max_done, max_step, shift_done = sem("logits_done"), sem("max_done"), sem("max_step"), sem("shift_done")
        shifted, exp_done, sum_done, den_done = sem("shifted"), sem("exp_done"), sem("sum_done"), sem("den_done")
        inv_done = sem("inv_done")
        mix_ready = [sem(f"mix_ready{n}") for n in range(2)]
        mix_out = [sem(f"mix_out{n}") for n in range(2)]
        o_ps, o_done, y_ps, y_done = sem("o_ps"), sem("o_done"), sem("y_ps"), sem("y_done")
        x_copied, scattered = sem("x_copied"), sem("scattered")

        block = stack.enter_context(nc.Block())

        @block.sync
        def _(sp):
            def load_cols(b, n):
                sp.dma_start(ctx_c[n][:, :, :, :], ctx_cols[b, :, :, :, :]).then_inc(ctx_c_in[n], 16)

            def load_rows(b, n):
                sp.dma_start(ctx_r[n][0:CTX_MAIN, :, :], ctx_rows[b, 0:CTX_MAIN, :, :]).then_inc(ctx_r_in[n], 16)
                sp.dma_start(ctx_r[n][CTX_MAIN:S_P, :, :], ctx_rows[b, CTX_MAIN:S_P, :, :]).then_inc(ctx_r_in[n], 16)

            def load_x(b0, b1):
                for b in range(b0, b1):
                    sp.dma_start(x_sb[:, b, :, :], x_pairs[:, b, :, :]).then_inc(x_in[b], 16)

            def copy_x(b):
                sp.dma_start(out_pairs[:, b, :, :], x_sb[:, b, :, :]).then_inc(x_copied, 16)

            load_x(*GROUPS[0])
            sp.dma_start(wq_sb[:, :, :], wq).then_inc(wq_in, 16)
            sp.dma_start(wk_sb[:, :, :], wk).then_inc(wk_in, 16)
            load_x(GROUPS[1][0], GROUPS[1][0] + 2)
            sp.wait_ge(gathered[0], 16)
            load_cols(0, 0)
            load_cols(1, 1)
            load_x(GROUPS[1][0] + 2, B)
            load_rows(0, 0)
            load_rows(1, 1)
            for b in range(B):
                sp.wait_ge(x_in[b], 16)
            with sp.Fori(0, B // 2 - 1) as i:
                for n in range(2):
                    b = i * 2 + (2 + n)
                    sp.wait_ge(logits_done, i * 2 + (1 + n))
                    load_cols(b, n)
                    sp.wait_ge(mix_ready[1], i * 2 + (1 + n))
                    load_rows(b, n)
                    copy_x(i * 2 + n)
            copy_x(B - 2)
            copy_x(B - 1)
            sp.dma_start(wv_sb[:, :, :], wv).then_inc(wv_in, 16)
            sp.dma_start(wo_sb[:, :, :], wo).then_inc(wo_in, 16)
            sp.wait_ge(scattered, 16)

        @block.gpsimd
        def _(pool):
            pool.memset(ident[:, :], 0.0).then_inc(consts_cleared, 1)
            pool.memset(own_batch[:, :, :], 0.0).then_inc(consts_cleared, 1)
            pool.memset(idx_diag[:, :, :], 0.0).then_inc(consts_done, 1)
            pool.wait_ge(consts_cleared, 2)
            pool.affine_select(out=ident[:, :], in_=ident[:, :], compare_op=ALU.not_equal, fill=1.0,
                               base=0, pattern=[[-1, P]], channel_multiplier=1).then_inc(consts_done, 1)
            pool.affine_select(out=own_batch[:, :, :], in_=own_batch[:, :, :], compare_op=ALU.not_equal, fill=1.0,
                               base=0, pattern=[[-1, GB], [0, TOPK]], channel_multiplier=1).then_inc(consts_done, 1)
            pool.iota(row_base_i[:, :], pattern=[[GROUPS[1][0] * N, len(GROUPS)]], base=0, channel_multiplier=N)\
                .then_inc(consts_done, 1)

            def gather(g):
                pool.wait_ge(idx_ready, g + 1)
                pool.indirect_dma_start(out=picked[g][:, :], out_offset=None, in_=x_rows,
                                        in_offset=bass.IndirectOffsetOnAxis(ap=row_idx[g][:, 0:1], axis=0))\
                    .then_inc(gathered[g], 16)

            gather(0)
            for b in range(B):
                if b in (GROUPS[0][0], GROUPS[1][0]):
                    pool.wait_ge(qk_done, QK_UNITS if b < GROUPS[1][0] else 2 * QK_UNITS)
                pool.wait_ge(max_done, b + 1)
                pool.wait_ge(shifted, b)
                pool.tensor_tensor(col_max[:, :], col_max[:, :], qk[0:S_P, b, DT, :], ALU.add).then_inc(max_step, 1)
                pool.wait_ge(max_step, b * 2 + 1)
                pool.partition_all_reduce(all_max[:, :], col_max[:, :], S_P, RMAX).then_inc(max_step, 1)
                pool.wait_ge(max_step, b * 2 + 2)
                pool.tensor_tensor(shift[:, :], qk[0:S_P, b, DT, :], all_max[:, :], ALU.subtract).then_inc(shift_done, 1)
                if b == 1:
                    gather(1)
            pool.wait_ge(x_copied, 16 * B)
            pool.wait_ge(y_done, 2)
            pool.indirect_dma_start(out=out_rows, out_offset=bass.IndirectOffsetOnAxis(ap=row_idx[1][:, 0:1], axis=0),
                                    in_=y_sb[:, :], in_offset=None).then_inc(scattered, 16)

        @block.scalar
        def _(act):
            act.dma_start(score_w_sb[:, :], score_w.broadcast_to([X_P, D])).then_inc(score_w_in, 16)
            act.dma_start(score_b_sb[:, :], score_b.broadcast_to([GB, 1])).then_inc(score_b_in, 16)
            act.dma_start(bias_sb[:, :, :], in_bias).then_inc(bias_in, 16)

            def copy_queries(g):
                b0, b1 = GROUPS[g]
                act.wait_ge(picked_T_ps, g + 1)
                nc.scalar.activation(picked_T[g][:, :, :], misc_ps[1][:, 0:DT * b1 * TOPK]
                                     .rearrange("p (t q) -> p t q", t=DT), ACT.Copy).then_inc(picked_T_done, 1)
                for u in range(QK_UNITS):
                    half, step = u // QK_STEPS, u % QK_STEPS
                    act.wait_ge(qk_ps, g * QK_UNITS + u + 1)
                    nc.scalar.activation(
                        qk[:, b0:b1, step, half * (HQ // 2):(half + 1) * (HQ // 2)].rearrange("p b (e c) -> p e b c", e=2),
                        fold_ps[u % 4][:, 0:HQ // 2 * (b1 - b0)].rearrange("p (e b c) -> p e b c", e=2, b=b1 - b0),
                        ACT.Copy).then_inc(qk_done, 1)

            def exponential(b, n):
                act.wait_ge(shifted, b + 1)
                nc.scalar.activation(probs[n][:, :, :], probs[n][:, :, :], ACT.Exp, scale=SCALE).then_inc(exp_done, 1)

            copy_queries(0)
            act.dma_start(out_b_sb[:, :], out_b.broadcast_to([BQ, D])).then_inc(out_b_in, 16)
            exponential(0, 0)
            exponential(1, 1)
            copy_queries(1)
            with act.Fori(1, B // 2) as i:
                exponential(i * 2, 0)
                exponential(i * 2 + 1, 1)

        @block.vector
        def _(dve):
            def score(b):
                dve.wait_ge(x_in[b], 16)
                for j in range(2):
                    if b:
                        dve.wait_ge(scored, 2 * b + j - 1)
                    nc.vector.tensor_tensor_reduce(
                        out=products[j][:, :], in0=x_sb[:, b, j, :], in1=score_w_sb[:, :], scale=1.0, scalar=0.0,
                        op0=ALU.mult, op1=ALU.add, accum_out=scores[:, j, b:b + 1]).then_inc(scored, 1)

            def link(ins, step):
                ins.then_inc(topk_step, 1)
                dve.wait_ge(topk_step, step)

            def choose_eight(g):
                nb = GROUPS[g][1] - GROUPS[g][0]
                dve.wait_ge(scores_T, g + 1)
                link(nc.vector.tensor_scalar(
                    score_rows[0:nb, :].rearrange("b (p j) -> b j p", j=2),
                    misc_ps[1][0:nb, 0:N].rearrange("b (j p) -> b j p", j=2), score_b_sb[0:nb, 0:1], None, ALU.add),
                    6 * g + 1)
                link(nc.vector.max(top[0:nb, 0:8], score_rows[0:nb, :]), 6 * g + 2)
                nc.vector.max_index(top_idx[0:nb, 0:8], top[0:nb, 0:8], score_rows[0:nb, :]).then_inc(topk_step, 1)
                nc.vector.match_replace(score_rest[0:nb, :], top[0:nb, 0:8], score_rows[0:nb, :], LOWEST)\
                    .then_inc(topk_step, 1)

            def choose_rest(g):
                b0, b1 = GROUPS[g]
                nb = b1 - b0
                dve.wait_ge(topk_step, 6 * g + 4)
                link(nc.vector.max(top[0:nb, 8:16], score_rest[0:nb, :]), 6 * g + 5)
                link(nc.vector.max_index(top_idx[0:nb, 8:16], top[0:nb, 8:16], score_rest[0:nb, :]), 6 * g + 6)
                nc.vector.scalar_tensor_tensor(
                    out=idx_diag[0:nb, g, b0 * TOPK:b1 * TOPK].rearrange("p (b q) -> p b q", q=TOPK),
                    in0=top_idx[0:nb, 0:TOPK].unsqueeze(1).broadcast_to([nb, nb, TOPK]),
                    scalar=row_base[0:nb, g:g + 1], in1=own_batch[0:nb, 0:nb, :], op0=ALU.add, op1=ALU.mult)\
                    .then_inc(idx_diag_done, 1)

            def move_idx(g):
                dve.wait_ge(idx_moved, g + 1)
                nc.vector.tensor_copy(row_idx[g][:, :], misc_ps[1][0:GROUPS[g][1] * TOPK, N:N + 1]).then_inc(idx_ready, 1)

            def spread_queries(g):
                b0, b1 = GROUPS[g]
                nb = b1 - b0
                for half in range(2):
                    dve.wait_ge(q_ps, 2 * g + half + 1)
                    for h in range(HPT):
                        rows = slice(h * DH, (h + 1) * DH)
                        last = nc.vector.tensor_tensor(
                            q_diag[g][rows, 2 * half:2 * half + 2, :, h, :],
                            misc_ps[half][rows, 0:2 * nb * TOPK].rearrange("p (t b q) -> p t b q", t=2, b=nb),
                            bias_sb[rows, 0, 2 * half:2 * half + 2].unsqueeze(2).unsqueeze(3)
                            .broadcast_to([DH, 2, nb, TOPK]), ALU.add)
                    last.then_inc(q_done, 1)

            def tiles(n):
                return logits_ps[n][0:S_P, :, 0:BANK_T * HQ].rearrange("p k (t c) -> p k t c", t=BANK_T)

            def find_max(b, n):
                dve.wait_ge(logits_done, b + 1)
                nc.vector.tensor_reduce(col_max[:, :], tiles(n).rearrange("p k t c -> p c k t"), AX.XY, ALU.max)\
                    .then_inc(max_done, 1)

            def subtract_max(b, n, waits_mix):
                dve.wait_ge(shift_done, b + 1)
                if waits_mix:
                    dve.wait_ge(mix_ready[1], b - 1)
                nc.vector.tensor_tensor(
                    probs[n][:, :, :].rearrange("p (k t) c -> p k t c", k=2), tiles(n),
                    shift[:, :].unsqueeze(1).unsqueeze(2).broadcast_to([S_P, 2, BANK_T, HQ]), ALU.add)\
                    .then_inc(shifted, 1)

            def sum_probs(b, n, waits_den):
                dve.wait_ge(exp_done, b + 1)
                if waits_den:
                    dve.wait_ge(den_done, b - 1)
                nc.vector.tensor_reduce(prob_sum[n][:, :], probs[n][:, :, :].rearrange("p t c -> p c t"), AX.X, ALU.add)\
                    .then_inc(sum_done, 1)

            def invert(b):
                dve.wait_ge(den_done, b + 1)
                if not isinstance(b, int) or b:
                    dve.wait_ge(mix_out[1], b)
                nc.vector.reciprocal(inv_sum[:, :], misc_ps[0][:, 0:HQ]).then_inc(inv_done, 1)

            def normalise(b, half):
                dve.wait_ge(inv_done, b + 1)
                dve.wait_ge(mix_ready[half], b + 1)
                nc.vector.tensor_tensor(
                    mix[:, 2 * half:2 * half + 2, :, bass.ds(b * TOPK, TOPK)],
                    mix_ps[half][:, 0:2 * HQ].rearrange("p (t h q) -> p t h q", t=2, h=HEADS),
                    inv_sum[:, :].rearrange("p (h q) -> p h q", h=HEADS).unsqueeze(1).broadcast_to([P, 2, HEADS, TOPK]),
                    ALU.mult).then_inc(mix_out[half], 1)

            def batch(b, n, waits=True):
                find_max(b, n)
                subtract_max(b, n, waits)
                invert(b - 1)
                normalise(b - 1, 0)
                normalise(b - 1, 1)
                sum_probs(b, n, waits)

            def finish_heads():
                for e in range(DT):
                    dve.wait_ge(o_ps, e + 1)
                    nc.vector.tensor_tensor(o_T[:, e, :], heads_ps[e][:, 0:BQ],
                                            bias_sb[:, 2, e:e + 1].broadcast_to([P, BQ]), ALU.add).then_inc(o_done, 1)

            def finish_output():
                dve.wait_ge(out_b_in, 16)
                for half in range(2):
                    cols = slice(half * (D // 2), (half + 1) * (D // 2))
                    dve.wait_ge(y_ps, half + 1)
                    nc.vector.tensor_tensor(y_sb[:, cols], logits_ps[0][0:BQ, half, 0:D // 2], out_b_sb[:, cols],
                                            ALU.add).then_inc(y_done, 1)

            for g in range(len(GROUPS)):
                nc.vector.memset(q_diag[g][:, :, :, :, :], 0.0).then_inc(vec_consts, 1)
            nc.vector.memset(ones[:, :], 1.0).then_inc(vec_consts, 1)
            dve.wait_ge(consts_done, 4)
            nc.vector.tensor_copy(row_base[:, :], row_base_i[:, :]).then_inc(vec_consts, 1)
            dve.wait_ge(vec_consts, 4)
            dve.wait_ge(score_w_in, 16)
            score(0)
            score(1)
            dve.wait_ge(score_b_in, 16)
            choose_eight(0)
            choose_rest(0)
            move_idx(0)
            dve.wait_ge(bias_in, 16)
            nc.vector.tensor_copy(key_bias[:, :, :], bias_sb[:, 1, :].unsqueeze(2).broadcast_to([P, DT, P]))\
                .then_inc(vec_consts, 1)
            spread_queries(0)
            score(2)
            score(3)
            score(4)
            score(5)
            find_max(0, 0)
            score(6)
            score(7)
            subtract_max(0, 0, False)
            choose_eight(1)
            find_max(1, 1)
            choose_rest(1)
            sum_probs(0, 0, False)
            move_idx(1)
            subtract_max(1, 1, False)
            invert(0)
            normalise(0, 0)
            sum_probs(1, 1, False)
            normalise(0, 1)
            invert(1)
            normalise(1, 0)
            normalise(1, 1)
            spread_queries(1)
            find_max(2, 0)
            subtract_max(2, 0, True)
            sum_probs(2, 0, True)
            with dve.Fori(1, B // 2 - 1) as i:
                batch(i * 2 + 1, 1)
                batch(i * 2 + 2, 0)
            batch(B - 1, 1)
            invert(B - 1)
            normalise(B - 1, 0)
            normalise(B - 1, 1)
            finish_heads()
            finish_output()

        @block.tensor
        def _(pe):
            def keep_warm(n):
                for _ in range(n):
                    nc.tensor.matmul(logits_ps[1][:, 1, 0:P], ones[:, :], ones[:, :], start=True, stop=True)

            def transpose_scores(g):
                b0, b1 = GROUPS[g]
                pe.wait_ge(scored, 2 * b1)
                if g:
                    pe.wait_ge(qk_done, QK_UNITS)
                for j in range(2):
                    last = nc.tensor.transpose(misc_ps[1][0:b1 - b0, j * X_P:(j + 1) * X_P],
                                               scores[:, j, b0:b1], ident[0:X_P, 0:X_P])
                last.then_inc(scores_T, 1)

            def move_idx(g):
                pe.wait_ge(idx_diag_done, g + 1)
                for k in range(g + 1):
                    b0, b1 = GROUPS[k]
                    last = nc.tensor.matmul(misc_ps[1][0:GROUPS[g][1] * TOPK, N:N + 1],
                                            idx_diag[0:b1 - b0, k, 0:GROUPS[g][1] * TOPK], ones[0:b1 - b0, 0:1],
                                            start=(k == 0), stop=(k == g))
                last.then_inc(idx_moved, 1)

            def transpose_picked(g):
                nq = GROUPS[g][1] * TOPK
                pe.wait_ge(gathered[g], 16)
                if g:
                    pe.wait_ge(qk_done, g * QK_UNITS)
                for t in range(DT):
                    last = nc.tensor.transpose(misc_ps[1][:, t * nq:(t + 1) * nq], picked[g][:, t * P:(t + 1) * P],
                                               ident[0:nq, 0:nq])
                last.then_inc(picked_T_ps, 1)

            def project_queries(g):
                b0, b1 = GROUPS[g]
                nq = (b1 - b0) * TOPK
                pe.wait_ge(picked_T_done, g + 1)
                if g:
                    pe.wait_ge(inv_done, 2)
                for half in range(2):
                    for k in range(2):
                        e = 2 * half + k
                        for t in range(DT):
                            last = nc.tensor.matmul(misc_ps[half][:, k * nq:(k + 1) * nq], wq_sb[:, t, e * P:(e + 1) * P],
                                                    picked_T[g][:, t, b0 * TOPK:b1 * TOPK], start=(t == 0), stop=(t == DT - 1))
                    last.then_inc(q_ps, 1)

            def fold_keys(g):
                w = HPT * TOPK * (GROUPS[g][1] - GROUPS[g][0])
                pe.wait_ge(q_done, 2 * g + 1)
                for u in range(QK_UNITS):
                    half, step = u // QK_STEPS, u % QK_STEPS
                    if u >= 4:
                        pe.wait_ge(qk_done, g * QK_UNITS + u - 3)
                    elif u < 2 and g:
                        pe.wait_ge(mix_out[u], GROUPS[0][1])
                    if u == 3:
                        pe.wait_ge(q_done, 2 * g + 2)
                    for k in range(2):
                        e = 2 * half + k
                        keys = wk_sb[:, e, step * P:(step + 1) * P] if step < DT else key_bias[:, e, :]
                        last = nc.tensor.matmul(fold_ps[u % 4][:, k * w:(k + 1) * w], keys,
                                                q_diag[g][:, e, :, :, :].rearrange("p b h q -> p (b h q)"),
                                                start=True, stop=True)
                    last.then_inc(qk_ps, 1)

            def logits(b, n, use, waits_slot, between=None):
                pe.wait_ge(ctx_c_in[n], use * 16 + 16)
                if waits_slot:
                    pe.wait_ge(shifted, b - 1)
                for t in range(S_T):
                    for f in range(DT):
                        last = nc.tensor.matmul(
                            logits_ps[n][0:S_P, t // BANK_T, (t % BANK_T) * HQ:(t % BANK_T + 1) * HQ],
                            ctx_c[n][:, f, t, :], qk[:, b, f, :], start=(f == 0), stop=(f == DT - 1))
                    if between is not None and t == S_T // 2:
                        between()
                last.then_inc(logits_done, 1)

            def weigh(b, n, use, between=None):
                pe.wait_ge(ctx_r_in[n], use * 32 + 32)
                pe.wait_ge(exp_done, b + 1)
                for half in range(2):
                    if not isinstance(b, int) or b:
                        pe.wait_ge(mix_out[half], b)
                    for f in range(2):
                        for t in range(S_T):
                            c = (2 * half + f) * P
                            last = nc.tensor.matmul(mix_ps[half][:, f * HQ:(f + 1) * HQ], ctx_r[n][:, t, c:c + P],
                                                    probs[n][:, t, :], start=(t == 0), stop=(t == S_T - 1))
                    last.then_inc(mix_ready[half], 1)
                    if half == 0:
                        if between is not None:
                            between()
                        pe.wait_ge(sum_done, b + 1)
                        if not isinstance(b, int) or b:
                            pe.wait_ge(inv_done, b)
                        nc.tensor.matmul(misc_ps[0][:, 0:HQ], ones[0:S_P, :], prob_sum[n][:, :],
                                         start=True, stop=True).then_inc(den_done, 1)

            def project_values():
                pe.wait_ge(wv_in, 16)
                pe.wait_ge(shifted, B)
                pe.wait_ge(inv_done, B)
                for half in range(2):
                    pe.wait_ge(mix_out[half], B)
                    for e in range(DT):
                        for t in range(2 * half, 2 * half + 2):
                            for h in range(HPT):
                                c = e * P + h * DH
                                last = nc.tensor.matmul(heads_ps[e][h * DH:(h + 1) * DH, 0:BQ], wv_sb[:, t, c:c + DH],
                                                        mix[:, t, e * HPT + h, :],
                                                        start=(t == 0), stop=(t == DT - 1), skip_group_check=True)
                        if half:
                            last.then_inc(o_ps, 1)

            def project_output():
                for half in range(2):
                    cols = slice(half * (D // 2), (half + 1) * (D // 2))
                    for e in range(DT):
                        if half == 0:
                            pe.wait_ge(o_done, e + 1)
                        last = nc.tensor.matmul(logits_ps[0][0:BQ, half, 0:D // 2], o_T[:, e, :], wo_sb[:, e, cols],
                                                start=(e == 0), stop=(e == DT - 1))
                    last.then_inc(y_ps, 1)

            pe.wait_ge(consts_done, 4)
            pe.wait_ge(vec_consts, 3)
            keep_warm(WARM_SCORES)
            transpose_scores(0)
            keep_warm(WARM_CHOICE)
            move_idx(0)
            keep_warm(WARM_GATHER)
            transpose_picked(0)
            keep_warm(2)
            pe.wait_ge(wq_in, 16)
            project_queries(0)
            pe.wait_ge(wk_in, 16)
            pe.wait_ge(vec_consts, 5)
            fold_keys(0)
            keep_warm(2)
            pe.wait_ge(qk_done, QK_UNITS - 1)
            logits(0, 0, 0, False)
            logits(1, 1, 0, False, between=lambda: transpose_scores(1))
            weigh(0, 0, 0, between=lambda: move_idx(1))
            weigh(1, 1, 0, between=lambda: transpose_picked(1))
            project_queries(1)
            fold_keys(1)
            pe.wait_ge(qk_done, 2 * QK_UNITS - 1)
            pe.wait_ge(idx_ready, 2)
            logits(2, 0, 1, True)
            with pe.Fori(1, B // 2 - 1) as i:
                logits(i * 2 + 1, 1, i, True)
                weigh(i * 2, 0, i)
                logits(i * 2 + 2, 0, i + 1, True)
                weigh(i * 2 + 1, 1, i)
            logits(B - 1, 1, B // 2 - 1, True)
            weigh(B - 2, 0, B // 2 - 1)
            weigh(B - 1, 1, B // 2 - 1)
            project_values()
            pe.wait_ge(wo_in, 16)
            project_output()


def kernel(x, ctx_1024, L0_xattn_in_proj_w, L0_xattn_in_proj_b, L0_xattn_out_w, L0_xattn_out_b,
           L0_xattn_score_w, L0_xattn_score_b):
    import numpy as np
    import concourse.bacc as bacc
    from concourse.bass_utils import run_bass_kernel_spmd

    ctx = np.asarray(ctx_1024)
    in_w = np.asarray(L0_xattn_in_proj_w)

    def in_major(w):
        return w.reshape(D, DT, P).transpose(2, 1, 0)

    arrays = {
        "x": np.asarray(x),
        "ctx_rows": ctx.reshape(B, S_P, S_T, D),
        "ctx_cols": ctx.reshape(B, S_P, S_T, DT, P).transpose(0, 4, 3, 2, 1),
        "wq": in_major(in_w[0:D]),
        "wk": in_w[D:2 * D].reshape(DT, P, D).transpose(1, 0, 2),
        "wv": in_major(in_w[2 * D:3 * D]),
        "wo": in_major(np.asarray(L0_xattn_out_w)),
        "in_bias": np.asarray(L0_xattn_in_proj_b).reshape(3, DT, P).transpose(2, 0, 1),
        "out_b": np.asarray(L0_xattn_out_b).reshape(1, D),
        "score_w": np.asarray(L0_xattn_score_w).reshape(1, D),
        "score_b": np.asarray(L0_xattn_score_b).reshape(1, 1),
    }
    nc = bacc.Bacc("TRN2", target_bir_lowering=False, num_devices=1)
    feeds, args = {}, []
    for name, a in arrays.items():
        a = np.ascontiguousarray(a)
        feeds[name + "_dram"] = a
        args.append(nc.dram_tensor(name + "_dram", a.shape, mybir.dt.from_np(a.dtype), kind="ExternalInput").ap())
    out = nc.dram_tensor("out_dram", (B, N, D), F32, kind="ExternalOutput").ap()
    build(nc, *args, out)
    return run_bass_kernel_spmd(nc, [feeds], core_ids=[0]).results[0]["out_dram"]
```
